# Optimizing a Trainium2 kernel written in Bass

```python
import numpy as np
import jax
import jax.numpy as jnp

def _softmax(x, axis=-1):
    return jax.nn.softmax(x, axis=axis)

def _gelu(x):
    return jax.nn.gelu(x, approximate=True)

def _silu(x):
    return jax.nn.silu(x)

def _sigmoid(x):
    return jax.nn.sigmoid(x)

def _layernorm(x, axis=-1, eps=1e-05):
    m = jnp.mean(x, axis=axis, keepdims=True)
    v = jnp.var(x, axis=axis, keepdims=True)
    return (x - m) / jnp.sqrt(v + eps)

def _scatter_add(tgt, idx, src, axis=0):
    return tgt.at[idx].add(src)

def _segment_sum(src, seg, n):
    return jax.ops.segment_sum(src, seg, n)
kernel_name = 'mk_adj_preln_d1_adj_r2_dd5f58'

def setup_inputs(seed: int=0):
    np.random.seed(seed)
    _w = jnp.asarray

    def _rec_inputs():
        import jax
        import jax.numpy as jnp
        _gk = jax.random.key(seed)
        x = -0.0002928 + 1 * jax.random.normal(jax.random.fold_in(_gk, 1), (128, 128, 128), jnp.float32)
        _a = jax.random.bernoulli(jax.random.fold_in(_gk, 2), 0.03125, (128, 128, 128))
        adj = _a.astype(jnp.int32)
        return (x, adj)
    x, adj = _rec_inputs()

    def _L0_gnn_setup():
        import jax, jax.numpy as jnp
        import numpy as np
        OUT = 128
        NUM_LAYERS = 3

        def _gru_cell(inp, h, w_ih, w_hh, b_ih, b_hh):
            gi = inp @ w_ih.T + b_ih
            gh = h @ w_hh.T + b_hh
            i_r, i_z, i_n = jnp.split(gi, 3, axis=-1)
            h_r, h_z, h_n = jnp.split(gh, 3, axis=-1)
            r = jax.nn.sigmoid(i_r + h_r)
            z = jax.nn.sigmoid(i_z + h_z)
            n = jnp.tanh(i_n + r * h_n)
            return (1.0 - z) * n + z * h
        key = jax.random.key(seed)
        ks = jax.random.split(key, 8)
        B, N, D = (32, 256, 128)
        x = jax.random.normal(ks[0], (B, N, D), dtype=jnp.float32)
        adj = jax.random.randint(ks[1], (B, N, N), 0, 2, dtype=jnp.int32)
        s = 1.0 / np.sqrt(OUT)
        weight = jax.random.uniform(ks[2], (NUM_LAYERS, OUT, OUT), jnp.float32, -s, s)
        w_ih = jax.random.uniform(ks[3], (3 * OUT, OUT), jnp.float32, -s, s)
        w_hh = jax.random.uniform(ks[4], (3 * OUT, OUT), jnp.float32, -s, s)
        b_ih = jax.random.uniform(ks[5], (3 * OUT,), jnp.float32, -s, s)
        b_hh = jax.random.uniform(ks[6], (3 * OUT,), jnp.float32, -s, s)
        return {'x': x, 'adj': adj, 'weight': weight, 'w_ih': w_ih, 'w_hh': w_hh, 'b_ih': b_ih, 'b_hh': b_hh}
    _L0_gnn_all = _L0_gnn_setup()
    _L0_gnn_in = {k: v for k, v in _L0_gnn_all.items() if k in ('weight', 'w_ih', 'w_hh', 'b_ih', 'b_hh')}
    del _L0_gnn_all
    return {'x': x, 'adj': adj, 'L0_gnn_weight': _L0_gnn_in['weight'], 'L0_gnn_w_ih': _L0_gnn_in['w_ih'], 'L0_gnn_w_hh': _L0_gnn_in['w_hh'], 'L0_gnn_b_ih': _L0_gnn_in['b_ih'], 'L0_gnn_b_hh': _L0_gnn_in['b_hh']}

def reference(x, adj, L0_gnn_weight, L0_gnn_w_ih, L0_gnn_w_hh, L0_gnn_b_ih, L0_gnn_b_hh):
    import jax
    import jax.numpy as jnp

    def _L0_gnn_ref(x, adj, weight, w_ih, w_hh, b_ih, b_hh):
        import jax, jax.numpy as jnp
        import numpy as np
        OUT = 128
        NUM_LAYERS = 3

        def _gru_cell(inp, h, w_ih, w_hh, b_ih, b_hh):
            gi = inp @ w_ih.T + b_ih
            gh = h @ w_hh.T + b_hh
            i_r, i_z, i_n = jnp.split(gi, 3, axis=-1)
            h_r, h_z, h_n = jnp.split(gh, 3, axis=-1)
            r = jax.nn.sigmoid(i_r + h_r)
            z = jax.nn.sigmoid(i_z + h_z)
            n = jnp.tanh(i_n + r * h_n)
            return (1.0 - z) * n + z * h
        A = (adj != 0).astype(x.dtype)
        h = x
        L = weight.shape[0]
        for i in range(L):
            m = jnp.einsum('bnd,de->bne', h, weight[i])
            aggr = jnp.einsum('bst,bsd->btd', A, m)
            h = _gru_cell(aggr, h, w_ih, w_hh, b_ih, b_hh)
        return h
    h = jnp.maximum(_layernorm(x, axis=-1), 0.0)
    x = x + _L0_gnn_ref(h, adj, L0_gnn_weight, L0_gnn_w_ih, L0_gnn_w_hh, L0_gnn_b_ih, L0_gnn_b_hh)
    return x

_drawn_inputs = setup_inputs


def setup_inputs(seed=0):
    import zlib

    import numpy as np

    out = dict(_drawn_inputs(seed))
    spreads = {}
    factors = {}
    for name, (base, spread) in spreads.items():
        noise = np.random.default_rng([zlib.crc32(name.encode()), seed]).standard_normal(out[name].shape)
        drawn = base * np.exp(spread * noise) if base else spread * noise
        out[name] = jnp.asarray(drawn.astype(out[name].dtype))
    for name, factor in factors.items():
        out[name] = (out[name] * factor).astype(out[name].dtype)
    return out
```

```python
from contextlib import ExitStack

import concourse.bass as bass
from concourse import mybir

P = 128
QUAD = 4
TILE = QUAD * P
TILES = 4
LAYERS = 3
GATES = 3
STEPS = LAYERS * TILES
LEAD = 3
EPS = 1e-5
WSCALE = 256.0

STATS_AT = {3: 0, 6: 1, 9: 2, 11: 3}
APPLY_AT = {4: 0, 7: 1, 10: 2, 12: 3}
TURN_AT = {5: 0, 8: 1, 11: 2, 13: 3}
H32_AT = {6: 0, 9: 1, 12: 2, 14: 3}
CAST_AT = {8: 0, 9: 1, 10: 2, 11: 3}

HEAD, BODY, TAIL = range(3)


def live(kind, step):
    return step >= 0 if kind == HEAD else (step < STEPS if kind == TAIL else True)


def gnn_program(nc, x, adj, weight, w_ih, w_hh, b_ih, b_hh, out):
    f32, f16, i32 = mybir.dt.float32, mybir.dt.float16, mybir.dt.int32
    ALU, ACT = mybir.AluOpType, mybir.ActivationFunctionType
    graphs = x.shape[0]
    batches = graphs // (TILES * QUAD)

    x_dram = x.rearrange("(b j q) n d -> b j n q d", j=TILES, q=QUAD)
    adj_dram = adj.rearrange("(b j q) s t -> b j s q t", j=TILES, q=QUAD)
    out_dram = out.rearrange("(b j q) n d -> b j n q d", j=TILES, q=QUAD)

    with ExitStack() as ctx:
        def sbuf(name, shape, dtype=f32):
            return ctx.enter_context(nc.sbuf_tensor(name, [P, *shape], dtype))

        def psum(name, shape, dtype=f32):
            return ctx.enter_context(nc.psum_tensor(name, [P, *shape], dtype))

        def sem(name):
            return ctx.enter_context(nc.semaphore(name))

        x_all = sbuf("x_all", [graphs * P])
        adj_raw = sbuf("adj_raw", [TILES, TILE], i32)
        adj16 = sbuf("adj16", [TILES, QUAD, P], f16)
        nat = sbuf("nat", [LAYERS, TILES, 2, TILE], f16)
        hT = sbuf("hT", [LAYERS, TILES, 2, TILE], f16)
        h32 = sbuf("h32", [LAYERS, TILES, TILE])
        place = (0, 1, 2, 1)
        aggT = sbuf("aggT", [2, 2, TILE], f16)
        r_buf = sbuf("r_buf", [2, TILE])
        z_buf = sbuf("z_buf", [2, TILE])
        n_buf = sbuf("n_buf", [2, TILE])
        d_buf = sbuf("d_buf", [2, TILE])
        normed = sbuf("normed", [TILE])
        stats = sbuf("stats", [QUAD, 6])
        mean_var = sbuf("mean_var", [2, QUAD, 2])
        var_eps = sbuf("var_eps", [QUAD])
        rstd = sbuf("rstd", [2, QUAD])
        minus_half = sbuf("minus_half", [QUAD])
        eps = sbuf("eps", [QUAD])
        w_raw = sbuf("w_raw", [LAYERS, P])
        wih_raw = sbuf("wih_raw", [GATES, P])
        whh_raw = sbuf("whh_raw", [GATES, P])
        wT = sbuf("wT", [LAYERS, P])
        wihT = sbuf("wihT", [GATES * P])
        whh = sbuf("whh", [2, GATES * P], f16)
        wgi = sbuf("wgi", [LAYERS, 2, GATES * P], f16)
        bias_i = sbuf("bias_i", [GATES])
        bias_h = sbuf("bias_h", [GATES])
        bias_rz = sbuf("bias_rz", [2])
        bias_hn = sbuf("bias_hn", [1])
        ident32 = sbuf("ident32", [P])
        ident16 = sbuf("ident16", [P], f16)

        r_ps = psum("r_ps", [TILE])
        z_ps = psum("z_ps", [TILE])
        hn_ps = psum("hn_ps", [TILE])
        in_ps = psum("in_ps", [TILE])
        agg_ps = psum("agg_ps", [TILE])
        turn_ps = psum("turn_ps", [2, TILE], f16)
        first_ps = psum("first_ps", [2, TILE], f16)
        out_ps = psum("out_ps", [TILE])

        x_loaded = [sem(f"x_loaded{j}") for j in range(TILES)]
        adj_loaded = [sem(f"adj_loaded{j}") for j in range(TILES)]
        weights_loaded = sem("weights_loaded")
        out_stored = sem("out_stored")
        r_made, z_made, hn_made, in_made = sem("r_made"), sem("z_made"), sem("hn_made"), sem("in_made")
        agg_made, turned, out_turned, first_turned = (
            sem("agg_made"), sem("turned"), sem("out_turned"), sem("first_turned"))
        w_turned, w_folded = sem("w_turned"), sem("w_folded")
        r_ready, z_ready, n_ready, hi_ready = sem("r_ready"), sem("z_ready"), sem("n_ready"), sem("hi_ready")
        agg_hi_ready, nat_ready = sem("agg_hi_ready"), sem("nat_ready")
        first_hi_ready, first_T_ready = sem("first_hi_ready"), sem("first_T_ready")
        whi_ready = sem("whi_ready")
        rgh_ready, pre_n_ready, h32_ready, lo_ready = (
            sem("rgh_ready"), sem("pre_n_ready"), sem("h32_ready"), sem("lo_ready"))
        agg_lo_ready, added, adj_ready = sem("agg_lo_ready"), sem("added"), sem("adj_ready")
        stats_made, moments_ready, normed_ready, first_lo_ready = (
            sem("stats_made"), sem("moments_ready"), sem("normed_ready"), sem("first_lo_ready"))
        w_copied, wlo_ready, bias_ready = sem("w_copied"), sem("wlo_ready"), sem("bias_ready")
        const_made, ident_made = sem("const_made"), sem("ident_made")
        eps_added, rstd_ready = sem("eps_added"), sem("rstd_ready")
        d_ready, zd_ready, first_h32_ready = sem("d_ready"), sem("zd_ready"), sem("first_h32_ready")

        block = ctx.enter_context(nc.Block())

        def steps_to(b, t):
            return b * STEPS + (t + 1)

        def turns_to(b, t):
            full, u = divmod(t, STEPS)
            return b * (2 * TILES) + (full * 2 * TILES + u + 1)

        def tiles_to(b, j):
            return b * TILES + (j + 1)

        def loads_to(b):
            return b * 16 + 16

        def wait(eng, semaphore, value):
            if not isinstance(value, int) or value > 0:
                eng.wait_ge(semaphore, value)

        def layer_tile(step):
            return step % STEPS // TILES, step % TILES

        def x_tile(b, j):
            return x_all[:, bass.ds(b * (TILES * TILE) + j * TILE, TILE)]

        @block.sync
        def _(sp):
            def load_x(b, j):
                sp.dma_start(x_tile(b, j).rearrange("p (q d) -> p q d", q=QUAD),
                             x_dram[b, j]).then_inc(x_loaded[j], 16)

            def load_adj(b, j):
                sp.dma_start(adj_raw[:, j, :].rearrange("p (q t) -> p q t", q=QUAD),
                             adj_dram[b, j]).then_inc(adj_loaded[j], 16)

            def next_x(b, j):
                sp.wait_ge(moments_ready, tiles_to(b + 1, j))
                load_x(b + 2, j)

            def next_adj(b, j):
                sp.wait_ge(adj_ready, tiles_to(b + 1, j))
                load_adj(b + 2, j)

            def store(b, j):
                sp.wait_ge(added, tiles_to(b, j))
                sp.dma_start(out_dram[b, j],
                             x_tile(b, j).rearrange("p (q d) -> p q d", q=QUAD)).then_inc(out_stored, 16)

            load_x(0, 0)
            load_adj(0, 0)
            sp.dma_start(w_raw[:, :, :], weight.rearrange("l d e -> d l e")).then_inc(weights_loaded, 16)
            sp.dma_start(wih_raw[:, :, :], w_ih.rearrange("(c g) e -> g c e", c=GATES)).then_inc(weights_loaded, 16)
            sp.dma_start(whh_raw[:, :, :], w_hh.rearrange("(c g) e -> g c e", c=GATES)).then_inc(weights_loaded, 16)
            with nc.allow_non_contiguous_dma("two vectors of 384 values"):
                sp.dma_start(bias_i[:, :], b_ih.rearrange("(c g) -> g c", c=GATES)).then_inc(weights_loaded, 16)
                sp.dma_start(bias_h[:, :], b_hh.rearrange("(c g) -> g c", c=GATES)).then_inc(weights_loaded, 16)
            for j in range(1, TILES):
                load_x(0, j)
                load_adj(0, j)
            for j in range(TILES):
                sp.wait_ge(moments_ready, tiles_to(0, j))
                load_x(1, j)
                sp.wait_ge(adj_ready, tiles_to(0, j))
                load_adj(1, j)
            with sp.Fori(0, batches - 2) as b:
                next_x(b, 0)
                next_x(b, 1)
                next_adj(b, 0)
                next_x(b, 2)
                next_adj(b, 1)
                store(b, 0)
                next_adj(b, 2)
                next_x(b, 3)
                store(b, 1)
                next_adj(b, 3)
                store(b, 2)
                store(b, 3)
            for b in (batches - 2, batches - 1):
                for j in range(TILES):
                    store(b, j)
            sp.wait_ge(out_stored, 16 * batches * TILES)

        @block.tensor
        def _(pe):
            def gate(ps, parts, made=None):
                n = 0
                for w, h, c, waits in parts:
                    for semaphore, value in waits:
                        wait(pe, semaphore, value)
                    for wp, hp in ((0, 0), (0, 1), (1, 0)):
                        last = nc.tensor.matmul(ps[:, :], w[:, wp, c * P:(c + 1) * P], h[:, hp, :],
                                                start=(n == 0), stop=(n == 3 * len(parts) - 1))
                        n += 1
                last.then_inc(made, 1)

            def aggregate(b, t):
                l, j = layer_tile(t)
                if l == 0:
                    pe.wait_ge(adj_ready, tiles_to(b, t // STEPS * TILES + j))
                    pe.wait_ge(first_lo_ready, tiles_to(b, t // STEPS * TILES + j))
                else:
                    pe.wait_ge(nat_ready, turns_to(b, t - TILES))
                wait(pe, agg_lo_ready, steps_to(b, t - 1))
                for q in range(QUAD):
                    for part in range(2):
                        last = nc.tensor.matmul(agg_ps[:, q * P:(q + 1) * P],
                                                nat[:, l, j, part, q * P:(q + 1) * P],
                                                adj16[:, j, q, :], start=(part == 0), stop=(part == 1))
                last.then_inc(agg_made, 1)

            def turn_first(b, j):
                pe.wait_ge(first_lo_ready, tiles_to(b, j))
                wait(pe, first_T_ready, tiles_to(b, j - 1))
                for part in range(2):
                    for q in range(QUAD):
                        cols = slice(q * P, (q + 1) * P)
                        last = nc.tensor.transpose(first_ps[:, part, cols], nat[:, 0, j, part, cols],
                                                   ident16[:, :])
                last.then_inc(first_turned, 1)

            def turn(b, t):
                l, j = layer_tile(t)
                pe.wait_ge(lo_ready, steps_to(b, t))
                source = hT[:, place[l + 1], j]
                if l + 1 < LAYERS:
                    wait(pe, nat_ready, turns_to(b, t) - 1)
                    for part in range(2):
                        for q in range(QUAD):
                            cols = slice(q * P, (q + 1) * P)
                            last = nc.tensor.transpose(turn_ps[:, part, cols], source[:, part, cols],
                                                       ident16[:, :])
                    last.then_inc(turned, 1)
                else:
                    if j:
                        pe.wait_ge(added, tiles_to(b, j - 1))
                    for q in range(QUAD):
                        cols = slice(q * P, (q + 1) * P)
                        for part in range(2):
                            last = nc.tensor.matmul(out_ps[:, cols], source[:, part, cols], ident16[:, :],
                                                    start=(part == 0), stop=(part == 1))
                    last.then_inc(out_turned, 1)

            def slot(kind, b, t):
                if live(kind, t):
                    l, j = layer_tile(t)
                    state = hT[:, l, j]
                    if l == 0:
                        h_waits = [(first_T_ready, tiles_to(b, t // STEPS * TILES + j))]
                    else:
                        h_waits = [(lo_ready, steps_to(b, t - TILES))]
                    agg_waits = [(agg_lo_ready, steps_to(b, t))]
                    wi, agg = wgi[:, l], aggT[:, t % 2]
                    wait(pe, r_ready, steps_to(b, t - 1))
                    gate(r_ps, [(whh, state, 0, h_waits), (wi, agg, 0, agg_waits)], r_made)
                    wait(pe, rgh_ready, steps_to(b, t - 1))
                    gate(hn_ps, [(whh, state, 2, [])], hn_made)
                if live(kind, t - 2):
                    turn(b, t - 2)
                if kind == BODY and t in TURN_AT:
                    turn_first(b + 1, TURN_AT[t])
                if live(kind, t):
                    wait(pe, pre_n_ready, steps_to(b, t - 1))
                    gate(in_ps, [(wi, agg, 2, [])], in_made)
                if live(kind, t + 1):
                    aggregate(b, t + 1)
                if live(kind, t):
                    wait(pe, z_ready, steps_to(b, t - 1))
                    gate(z_ps, [(whh, state, 1, []), (wi, agg, 1, [])], z_made)

            pe.wait_ge(weights_loaded, 80)
            pe.wait_ge(ident_made, 2)
            for source, target in ((wih_raw, r_ps), (w_raw, z_ps), (whh_raw, hn_ps)):
                for c in range(3):
                    last = nc.tensor.transpose(target[:, c * P:(c + 1) * P], source[:, c, :], ident32[:, :])
                last.then_inc(w_turned, 1)
            pe.wait_ge(w_copied, 2)
            pe.wait_ge(ident_made, 3)
            pe.wait_ge(wlo_ready, 1)
            for l, target in enumerate((in_ps, agg_ps, hn_ps)):
                nc.tensor.matmul(target[:, 0:GATES * P], wT[:, l, :], wihT[:, :],
                                 start=True, stop=True).then_inc(w_folded, 1)
            turn_first(0, 0)
            pe.wait_ge(wlo_ready, 4)
            aggregate(0, 0)
            turn_first(0, 1)
            slot(HEAD, 0, 0)
            turn_first(0, 2)
            slot(HEAD, 0, 1)
            turn_first(0, 3)
            slot(HEAD, 0, 2)
            with pe.Fori(0, batches - 1) as b:
                for t in range(LEAD, LEAD + STEPS):
                    slot(BODY, b, t)
            for t in range(LEAD, LEAD + STEPS):
                slot(TAIL, batches - 1, t)

        @block.scalar
        def _(act):
            def first_hi(b, j):
                act.wait_ge(normed_ready, tiles_to(b, j))
                nc.scalar.activation(nat[:, 0, j, 0, :], normed[:, :], ACT.Relu).then_inc(first_hi_ready, 1)

            def first_T(b, j):
                act.wait_ge(first_turned, tiles_to(b, j))
                nc.scalar.activation(hT[:, 0, j], first_ps[:, :, :], ACT.Copy).then_inc(first_T_ready, 1)

            def agg_hi(b, t):
                act.wait_ge(agg_made, steps_to(b, t))
                nc.scalar.activation(aggT[:, t % 2, 0, :], agg_ps[:, :], ACT.Copy).then_inc(agg_hi_ready, 1)

            def slot(kind, b, t):
                if live(kind, t - 1):
                    act.wait_ge(z_made, steps_to(b, t - 1))
                    nc.scalar.activation(z_buf[:, (t - 1) % 2, :], z_ps[:, :], ACT.Sigmoid,
                                         bias=bias_rz[:, 1:2], scale=1 / WSCALE).then_inc(z_ready, 1)
                if live(kind, t):
                    act.wait_ge(r_made, steps_to(b, t))
                    nc.scalar.activation(r_buf[:, t % 2, :], r_ps[:, :], ACT.Sigmoid,
                                         bias=bias_rz[:, 0:1], scale=1 / WSCALE).then_inc(r_ready, 1)
                if kind == BODY and t in APPLY_AT:
                    first_hi(b + 1, APPLY_AT[t])
                if live(kind, t - 2) and layer_tile(t - 2)[0] + 1 < LAYERS:
                    l, j = layer_tile(t - 2)
                    act.wait_ge(turned, turns_to(b, t - 2))
                    nc.scalar.activation(nat[:, l + 1, j], turn_ps[:, :, :], ACT.Copy).then_inc(nat_ready, 1)
                if live(kind, t - 1):
                    l, j = layer_tile(t - 1)
                    act.wait_ge(h32_ready, steps_to(b, t - 1))
                    nc.scalar.activation(hT[:, place[l + 1], j, 0, :], h32[:, place[l + 1], j, :],
                                         ACT.Copy).then_inc(hi_ready, 1)
                if live(kind, t + 1):
                    agg_hi(b, t + 1)
                if live(kind, t):
                    act.wait_ge(pre_n_ready, steps_to(b, t))
                    nc.scalar.activation(n_buf[:, t % 2, :], r_buf[:, t % 2, :], ACT.Tanh,
                                         bias=bias_i[:, 2:3], scale=1 / WSCALE).then_inc(n_ready, 1)
                if kind == BODY and t in TURN_AT:
                    first_T(b + 1, TURN_AT[t])

            first_hi(0, 0)
            act.wait_ge(w_turned, 3)
            nc.scalar.activation(whh[:, 0, :], hn_ps[:, 0:GATES * P], ACT.Copy, scale=WSCALE).then_inc(whi_ready, 1)
            for l, source in enumerate((in_ps, agg_ps, hn_ps)):
                act.wait_ge(w_folded, l + 1)
                nc.scalar.activation(wgi[:, l, 0, :], source[:, 0:GATES * P], ACT.Copy,
                                     scale=WSCALE).then_inc(whi_ready, 1)
            first_T(0, 0)
            first_hi(0, 1)
            agg_hi(0, 0)
            first_T(0, 1)
            act.wait_ge(bias_ready, 1)
            slot(HEAD, 0, 0)
            first_hi(0, 2)
            first_T(0, 2)
            slot(HEAD, 0, 1)
            first_hi(0, 3)
            first_T(0, 3)
            slot(HEAD, 0, 2)
            with act.Fori(0, batches - 1) as b:
                for t in range(LEAD, LEAD + STEPS):
                    slot(BODY, b, t)
            for t in range(LEAD, LEAD + STEPS):
                slot(TAIL, batches - 1, t)

        @block.vector
        def _(dve):
            def half_moments(b, j):
                dve.wait_ge(x_loaded[j], loads_to(b))
                for q in range(QUAD):
                    last = nc.vector.bn_stats(stats[:, q, :], x_all[:, bass.ds(b * (TILES * TILE) + (j * TILE + q * P), P)])
                last.then_inc(stats_made, 1)

            def moments(j):
                for q in range(QUAD):
                    last = nc.vector.bn_aggr(mean_var[:, j % 2, q, :], stats[:, q, :])
                last.then_inc(moments_ready, 1)

            def norm(b, j):
                dve.wait_ge(rstd_ready, tiles_to(b, j))
                for q in range(QUAD):
                    last = nc.vector.tensor_scalar(
                        normed[:, q * P:(q + 1) * P],
                        x_all[:, bass.ds(b * (TILES * TILE) + (j * TILE + q * P), P)],
                        mean_var[:, j % 2, q, 0:1], rstd[:, j % 2, q:q + 1], ALU.subtract, ALU.mult)
                last.then_inc(normed_ready, 1)

            def first_lo(b, j):
                dve.wait_ge(first_hi_ready, tiles_to(b, j))
                nc.vector.scalar_tensor_tensor(nat[:, 0, j, 1, :], normed[:, :], 0.0, nat[:, 0, j, 0, :],
                                               ALU.max, ALU.subtract).then_inc(first_lo_ready, 1)

            def cast_adj(b, j):
                dve.wait_ge(adj_loaded[j], loads_to(b))
                nc.vector.tensor_scalar(adj16[:, j, :, :].rearrange("p q t -> p (q t)"), adj_raw[:, j, :], 0.0, None,
                                        ALU.not_equal).then_inc(adj_ready, 1)

            def agg_lo(b, t):
                dve.wait_ge(agg_hi_ready, steps_to(b, t))
                nc.vector.tensor_tensor(aggT[:, t % 2, 1, :], agg_ps[:, :], aggT[:, t % 2, 0, :],
                                        ALU.subtract).then_inc(agg_lo_ready, 1)

            def slot(kind, b, t):
                if live(kind, t - 3) and layer_tile(t - 3)[0] + 1 == LAYERS:
                    j = layer_tile(t - 3)[1]
                    dve.wait_ge(out_turned, tiles_to(b, j))
                    nc.vector.tensor_tensor(x_tile(b, j), out_ps[:, :], x_tile(b, j), ALU.add).then_inc(added, 1)
                if kind == BODY and t in STATS_AT:
                    half_moments(b + 1, STATS_AT[t])
                if kind == BODY and t in APPLY_AT:
                    norm(b + 1, APPLY_AT[t])
                if kind == BODY and t in CAST_AT:
                    cast_adj(b + 1, CAST_AT[t])
                if kind == BODY and t in STATS_AT:
                    dve.wait_ge(stats_made, tiles_to(b + 1, STATS_AT[t]))
                if live(kind, t):
                    dve.wait_ge(r_ready, steps_to(b, t))
                    dve.wait_ge(hn_made, steps_to(b, t))
                    nc.vector.scalar_tensor_tensor(r_buf[:, t % 2, :], hn_ps[:, :], bias_hn[:, :], r_buf[:, t % 2, :],
                                                   ALU.add, ALU.mult).then_inc(rgh_ready, 1)
                if kind == BODY and t in STATS_AT:
                    moments(STATS_AT[t])
                if live(kind, t - 1):
                    l, j = layer_tile(t - 1)
                    dve.wait_ge(zd_ready, steps_to(b, t - 1))
                    nc.vector.tensor_tensor(h32[:, place[l + 1], j, :], n_buf[:, (t - 1) % 2, :],
                                            d_buf[:, (t - 1) % 2, :], ALU.add).then_inc(h32_ready, 1)
                if kind == BODY and t in APPLY_AT:
                    first_lo(b + 1, APPLY_AT[t])
                if live(kind, t):
                    dve.wait_ge(in_made, steps_to(b, t))
                    dve.wait_ge(rgh_ready, steps_to(b, t))
                    nc.vector.tensor_tensor(r_buf[:, t % 2, :], in_ps[:, :], r_buf[:, t % 2, :],
                                            ALU.add).then_inc(pre_n_ready, 1)
                if live(kind, t + 1):
                    agg_lo(b, t + 1)
                if live(kind, t - 1):
                    l, j = layer_tile(t - 1)
                    dve.wait_ge(hi_ready, steps_to(b, t - 1))
                    nc.vector.tensor_tensor(hT[:, place[l + 1], j, 1, :], h32[:, place[l + 1], j, :],
                                            hT[:, place[l + 1], j, 0, :], ALU.subtract).then_inc(lo_ready, 1)

            half_moments(0, 0)
            dve.wait_ge(stats_made, tiles_to(0, 0))
            moments(0)
            dve.wait_ge(ident_made, 2)
            nc.vector.tensor_copy(ident16[:, :], ident32[:, :]).then_inc(ident_made, 1)
            norm(0, 0)
            first_lo(0, 0)
            cast_adj(0, 0)
            dve.wait_ge(weights_loaded, 80)
            nc.vector.tensor_tensor(bias_rz[:, :], bias_i[:, 0:2], bias_h[:, 0:2], ALU.add)
            nc.vector.tensor_scalar(bias_hn[:, :], bias_h[:, 2:3], WSCALE, None, ALU.mult).then_inc(bias_ready, 1)
            dve.wait_ge(w_turned, 1)
            nc.vector.tensor_copy(wihT[:, :], r_ps[:, 0:GATES * P]).then_inc(w_copied, 1)
            dve.wait_ge(w_turned, 2)
            nc.vector.tensor_copy(wT[:, :, :], z_ps[:, 0:LAYERS * P].rearrange("p (l d) -> p l d", l=LAYERS)).then_inc(w_copied, 1)
            for n, (target, source) in enumerate(
                    [(whh, hn_ps)] + [(wgi[:, l], ps) for l, ps in enumerate((in_ps, agg_ps, hn_ps))]):
                dve.wait_ge(whi_ready, n + 1)
                nc.vector.scalar_tensor_tensor(target[:, 1, :], source[:, 0:GATES * P], WSCALE, target[:, 0, :],
                                               ALU.mult, ALU.subtract).then_inc(wlo_ready, 1)
            half_moments(0, 1)
            dve.wait_ge(stats_made, tiles_to(0, 1))
            moments(1)
            norm(0, 1)
            first_lo(0, 1)
            cast_adj(0, 1)
            agg_lo(0, 0)
            half_moments(0, 2)
            dve.wait_ge(stats_made, tiles_to(0, 2))
            moments(2)
            norm(0, 2)
            slot(HEAD, 0, 0)
            first_lo(0, 2)
            cast_adj(0, 2)
            half_moments(0, 3)
            dve.wait_ge(stats_made, tiles_to(0, 3))
            moments(3)
            norm(0, 3)
            slot(HEAD, 0, 1)
            first_lo(0, 3)
            cast_adj(0, 3)
            slot(HEAD, 0, 2)
            with dve.Fori(0, batches - 1) as b:
                for t in range(LEAD, LEAD + STEPS):
                    slot(BODY, b, t)
            for t in range(LEAD, LEAD + STEPS):
                slot(TAIL, batches - 1, t)

        @block.gpsimd
        def _(pool):
            def inverse_std(b, j):
                pool.wait_ge(moments_ready, tiles_to(b, j))
                nc.gpsimd.tensor_tensor(var_eps[:, :], mean_var[:, j % 2, :, 1], eps[:, :],
                                        ALU.add).then_inc(eps_added, 1)
                pool.wait_ge(eps_added, tiles_to(b, j))
                nc.gpsimd.tensor_tensor(rstd[:, j % 2, :], var_eps[:, :], minus_half[:, :],
                                        ALU.pow).then_inc(rstd_ready, 1)

            def first_h32(b, j):
                pool.wait_ge(first_T_ready, tiles_to(b, j))
                nc.gpsimd.tensor_tensor(h32[:, 0, j, :], hT[:, 0, j, 0, :], hT[:, 0, j, 1, :],
                                        ALU.add).then_inc(first_h32_ready, 1)

            def slot(kind, b, t):
                if live(kind, t - 1):
                    pool.wait_ge(z_ready, steps_to(b, t - 1))
                    pool.wait_ge(d_ready, steps_to(b, t - 1))
                    p = (t - 1) % 2
                    nc.gpsimd.tensor_tensor(d_buf[:, p, :], z_buf[:, p, :], d_buf[:, p, :],
                                            ALU.mult).then_inc(zd_ready, 1)
                if kind == BODY and t in STATS_AT:
                    inverse_std(b + 1, STATS_AT[t])
                if kind == BODY and t in H32_AT:
                    first_h32(b + 1, H32_AT[t])
                if live(kind, t):
                    l, j = layer_tile(t)
                    pool.wait_ge(n_ready, steps_to(b, t))
                    if l == 0:
                        pool.wait_ge(first_h32_ready, tiles_to(b, t // STEPS * TILES + j))
                    wait(pool, h32_ready, steps_to(b, t - 2))
                    nc.gpsimd.tensor_tensor(d_buf[:, t % 2, :], h32[:, l, j, :], n_buf[:, t % 2, :],
                                            ALU.subtract).then_inc(d_ready, 1)

            nc.gpsimd.memset(ident32[:, :], 0.0).then_inc(ident_made, 1)
            pool.wait_ge(ident_made, 1)
            nc.gpsimd.affine_select(out=ident32[:, :], in_=ident32[:, :], compare_op=ALU.not_equal, fill=1.0,
                                    base=0, pattern=[[-1, P]], channel_multiplier=1).then_inc(ident_made, 1)
            nc.gpsimd.memset(minus_half[:, :], -0.5).then_inc(const_made, 1)
            nc.gpsimd.memset(eps[:, :], EPS).then_inc(const_made, 1)
            pool.wait_ge(const_made, 2)
            for j in range(TILES):
                inverse_std(0, j)
                if j == 1:
                    first_h32(0, 0)
                    first_h32(0, 1)
                if j == 2:
                    slot(HEAD, 0, 0)
            first_h32(0, 2)
            slot(HEAD, 0, 1)
            first_h32(0, 3)
            slot(HEAD, 0, 2)
            with pool.Fori(0, batches - 1) as b:
                for t in range(LEAD, LEAD + STEPS):
                    slot(BODY, b, t)
            for t in range(LEAD, LEAD + STEPS):
                slot(TAIL, batches - 1, t)


_INPUTS = ("x", "adj", "L0_gnn_weight", "L0_gnn_w_ih", "L0_gnn_w_hh", "L0_gnn_b_ih", "L0_gnn_b_hh")


def kernel(**inputs):
    import numpy as np
    import concourse.bacc as bacc
    from concourse.bass_utils import run_bass_kernel_spmd

    nc = bacc.Bacc("TRN2", target_bir_lowering=False, num_devices=1)
    arrays, args = {}, []
    for name in _INPUTS:
        a = np.ascontiguousarray(inputs[name])
        arrays[f"in_{name}"] = a
        args.append(nc.dram_tensor(f"in_{name}", a.shape, mybir.dt.from_np(a.dtype), kind="ExternalInput").ap())
    shape = arrays["in_x"].shape
    out = nc.dram_tensor("out", shape, mybir.dt.float32, kind="ExternalOutput").ap()
    gnn_program(nc, *args, out)
    result = run_bass_kernel_spmd(nc, [arrays], core_ids=[0])
    return result.results[0]["out"]
```

```python
from contextlib import ExitStack

import concourse.bass as bass
from concourse import mybir

P = 128
QUAD = 4
TILE = QUAD * P
TILES = 4
LAYERS = 3
GATES = 3
STEPS = LAYERS * TILES
LEAD = 3
EPS = 1e-5
WSCALE = 256.0

HEAD, BODY, TAIL = range(3)

X_LOAD_AT = {HEAD: {}, BODY: {3: 0, 5: 1, 7: 2, 9: 3}, TAIL: {}}
ADJ_LOAD_AT = {HEAD: {}, BODY: {4: 0, 5: 1, 6: 2, 7: 3}, TAIL: {}}
STATS_AT = {HEAD: {}, BODY: {4: 0, 6: 1, 8: 2, 10: 3}, TAIL: {}}
APPLY_AT = {HEAD: {0: 2, 1: 3}, BODY: {5: 0, 7: 1, 9: 2, 11: 3}, TAIL: {}}
CAST_AT = {HEAD: {0: 2, 1: 3}, BODY: {8: 0, 10: 1, 12: 2, 13: 3}, TAIL: {}}
H32_AT = {HEAD: {1: 2, 2: 3}, BODY: {7: 0, 9: 1, 11: 2, 13: 3}, TAIL: {}}


def live(kind, step):
    return step >= 0 if kind == HEAD else (step < STEPS if kind == TAIL else True)


def prepared(kind, b):
    return b + 1 if kind == BODY else b


def gnn_program(nc, x, adj, weight, w_ih, w_hh, b_ih, b_hh, out):
    f32, f16, i32 = mybir.dt.float32, mybir.dt.float16, mybir.dt.int32
    ALU, ACT = mybir.AluOpType, mybir.ActivationFunctionType
    graphs = x.shape[0]
    batches = graphs // (TILES * QUAD)

    x_dram = x.rearrange("(b j q) n d -> b j n q d", j=TILES, q=QUAD)
    adj_dram = adj.rearrange("(b j q) s t -> b j s q t", j=TILES, q=QUAD)
    out_dram = out.rearrange("(b j q) n d -> b j n q d", j=TILES, q=QUAD)

    with ExitStack() as ctx:
        def sbuf(name, shape, dtype=f32):
            return ctx.enter_context(nc.sbuf_tensor(name, [P, *shape], dtype))

        def psum(name, shape, dtype=f32):
            return ctx.enter_context(nc.psum_tensor(name, [P, *shape], dtype))

        def sem(name):
            return ctx.enter_context(nc.semaphore(name))

        x_all = sbuf("x_all", [graphs * P])
        adj_raw = sbuf("adj_raw", [TILES, TILE], i32)
        adj16 = sbuf("adj16", [TILES, QUAD, P], f16)
        nat = sbuf("nat", [LAYERS, TILES, 2, TILE], f16)
        hT = sbuf("hT", [LAYERS, TILES, 2, TILE], f16)
        h32 = sbuf("h32", [LAYERS, TILES, TILE])
        place = (0, 1, 2, 1)
        nat_place = (0, 1, 2, 2)
        aggT = sbuf("aggT", [2, 2, TILE], f16)
        r_buf = sbuf("r_buf", [2, TILE])
        z_buf = sbuf("z_buf", [2, TILE])
        n_buf = sbuf("n_buf", [2, TILE])
        d_buf = sbuf("d_buf", [2, TILE])
        normed = sbuf("normed", [2, TILE])
        stats = sbuf("stats", [2, QUAD, 6])
        mean_var = sbuf("mean_var", [2, QUAD, 2])
        var_eps = sbuf("var_eps", [2, QUAD])
        rstd = sbuf("rstd", [2, QUAD])
        minus_half = sbuf("minus_half", [QUAD])
        eps = sbuf("eps", [QUAD])
        warm = sbuf("warm", [1])
        w_raw = sbuf("w_raw", [LAYERS, P])
        wih_raw = sbuf("wih_raw", [GATES, P])
        whh_raw = sbuf("whh_raw", [GATES, P])
        wT = sbuf("wT", [LAYERS, P])
        wihT = sbuf("wihT", [GATES * P])
        whh = sbuf("whh", [2, GATES * P], f16)
        wgi = sbuf("wgi", [LAYERS, 2, GATES * P], f16)
        bias_i = sbuf("bias_i", [GATES])
        bias_h = sbuf("bias_h", [GATES])
        bias_rz = sbuf("bias_rz", [2])
        bias_hn = sbuf("bias_hn", [1])
        ident32 = sbuf("ident32", [P])
        ident16 = sbuf("ident16", [P], f16)

        r_ps = psum("r_ps", [TILE])
        z_ps = psum("z_ps", [TILE])
        hn_ps = psum("hn_ps", [TILE])
        in_ps = psum("in_ps", [TILE])
        agg_ps = psum("agg_ps", [TILE])
        fold_ps = psum("fold_ps", [2, TILE])
        out_ps = psum("out_ps", [TILE])

        x_loaded = [sem(f"x_loaded{j}") for j in range(TILES)]
        adj_loaded = [sem(f"adj_loaded{j}") for j in range(TILES)]
        first_T_ready = [sem(f"first_T_ready{j}") for j in range(TILES)]
        nat_ready = [sem(f"nat_ready{j}") for j in range(TILES)]
        weights_loaded, biases_loaded = sem("weights_loaded"), sem("biases_loaded")
        out_stored, turns_begun = sem("out_stored"), sem("turns_begun")
        r_made, z_made, hn_made, in_made = sem("r_made"), sem("z_made"), sem("hn_made"), sem("in_made")
        agg_made, out_turned = sem("agg_made"), sem("out_turned")
        w_turned, w_folded = sem("w_turned"), sem("w_folded")
        r_ready, z_ready, n_ready, hi_ready = sem("r_ready"), sem("z_ready"), sem("n_ready"), sem("hi_ready")
        agg_hi_ready, first_hi_ready = sem("agg_hi_ready"), sem("first_hi_ready")
        sign_made = sem("sign_made")
        w_copied, whi_ready = sem("w_copied"), sem("whi_ready")
        rgh_ready, pre_n_ready, h32_ready, lo_ready = (
            sem("rgh_ready"), sem("pre_n_ready"), sem("h32_ready"), sem("lo_ready"))
        hi_added = sem("hi_added")
        agg_lo_ready, added, adj_ready = sem("agg_lo_ready"), sem("added"), sem("adj_ready")
        stats_made, moments_ready, normed_ready, first_lo_ready = (
            sem("stats_made"), sem("moments_ready"), sem("normed_ready"), sem("first_lo_ready"))
        wlo_ready, bias_ready = sem("wlo_ready"), sem("bias_ready")
        const_made, ident_made = sem("const_made"), sem("ident_made")
        eps_added, rstd_ready = sem("eps_added"), sem("rstd_ready")
        d_ready, zd_ready, first_h32_ready = sem("d_ready"), sem("zd_ready"), sem("first_h32_ready")

        block = ctx.enter_context(nc.Block())

        def steps_to(b, t):
            return b * STEPS + (t + 1)

        def turns_to(b, step):
            return b * (LAYERS * 16) + (step // STEPS * LAYERS * 16 + layer_tile(step)[0] * 16 + 16)

        def tiles_to(b, j):
            return b * TILES + (j + 1)

        def loads_to(b):
            return b * 16 + 16

        def wait(eng, semaphore, value):
            if not isinstance(value, int) or value > 0:
                eng.wait_ge(semaphore, value)

        def layer_tile(step):
            return step % STEPS // TILES, step % TILES

        def x_tile(b, j):
            return x_all[:, bass.ds(b * (TILES * TILE) + j * TILE, TILE)]

        @block.sync
        def _(sp):
            def load_x(b, j):
                sp.dma_start(x_tile(b, j).rearrange("p (q d) -> p q d", q=QUAD),
                             x_dram[b, j]).then_inc(x_loaded[j], 16)

            def load_adj(b, j):
                sp.dma_start(adj_raw[:, j, :].rearrange("p (q t) -> p q t", q=QUAD),
                             adj_dram[b, j]).then_inc(adj_loaded[j], 16)

            def turn_first(b, j):
                sp.wait_ge(first_lo_ready, tiles_to(b, j))
                sp.sem_inc(turns_begun, 1)
                sp.dma_start_transpose(hT[:, 0, j].rearrange("p a (q n) -> p (a q) n", q=QUAD),
                                       nat[:, 0, j].rearrange("p a f -> p (a f)")).then_inc(first_T_ready[j], 16)

            def turn(b, t):
                l, j = layer_tile(t)
                sp.wait_ge(lo_ready, steps_to(b, t))
                sp.sem_inc(turns_begun, 1)
                sp.dma_start_transpose(nat[:, nat_place[l + 1], j].rearrange("p a (q n) -> p (a q) n", q=QUAD),
                                       hT[:, place[l + 1], j].rearrange("p a f -> p (a f)")).then_inc(nat_ready[j], 16)

            def store(b, j):
                sp.wait_ge(added, tiles_to(b, j))
                sp.dma_start(out_dram[b, j],
                             x_tile(b, j).rearrange("p (q d) -> p q d", q=QUAD)).then_inc(out_stored, 16)

            def slot(kind, b, t):
                if t in X_LOAD_AT[kind]:
                    load_x(b + 1, X_LOAD_AT[kind][t])
                if t in ADJ_LOAD_AT[kind]:
                    j = ADJ_LOAD_AT[kind][t]
                    sp.wait_ge(adj_ready, tiles_to(b, j))
                    load_adj(b + 1, j)
                if live(kind, t - 2) and not (kind == TAIL and layer_tile(t - 2)[0] + 1 == LAYERS):
                    turn(b, t - 2)
                if live(kind, t - 3) and layer_tile(t - 3)[0] + 1 == LAYERS:
                    store(b, layer_tile(t - 3)[1])
                if t in APPLY_AT[kind]:
                    turn_first(prepared(kind, b), APPLY_AT[kind][t])

            for j in (0, 1):
                load_x(0, j)
            for j in (0, 1):
                load_adj(0, j)
            for j in (2, 3):
                load_x(0, j)
            for j in (2, 3):
                load_adj(0, j)
            turn_first(0, 0)
            turn_first(0, 1)
            for t in range(LEAD):
                slot(HEAD, 0, t)
            with sp.Fori(0, batches - 1) as b:
                for t in range(LEAD, LEAD + STEPS):
                    slot(BODY, b, t)
            for t in range(LEAD, LEAD + STEPS):
                slot(TAIL, batches - 1, t)
            sp.wait_ge(out_stored, 16 * batches * TILES)

        @block.tensor
        def _(pe):
            def product(ps, w, h, c, first=True, last=True):
                nc.tensor.matmul(ps[:, :], w[:, 0, c * P:(c + 1) * P], h[:, 0, :], start=first, stop=False)
                nc.tensor.matmul(ps[:, :], w[:, 0, c * P:(c + 1) * P], h[:, 1, :], start=False, stop=False)
                return nc.tensor.matmul(ps[:, :], w[:, 1, c * P:(c + 1) * P], h[:, 0, :], start=False, stop=last)

            def aggregate(b, t):
                l, j = layer_tile(t)
                if l == 0:
                    pe.wait_ge(adj_ready, tiles_to(b, t // STEPS * TILES + j))
                    pe.wait_ge(first_lo_ready, tiles_to(b, t // STEPS * TILES + j))
                else:
                    pe.wait_ge(nat_ready[j], turns_to(b, t - TILES))
                wait(pe, agg_lo_ready, steps_to(b, t - 1))
                for q in range(QUAD):
                    for part in range(2):
                        last = nc.tensor.matmul(agg_ps[:, q * P:(q + 1) * P],
                                                nat[:, l, j, part, q * P:(q + 1) * P],
                                                adj16[:, j, q, :], start=(part == 0), stop=(part == 1))
                last.then_inc(agg_made, 1)

            def turn_out(b, j):
                pe.wait_ge(lo_ready, steps_to(b, STEPS - TILES + j))
                if j:
                    pe.wait_ge(added, tiles_to(b, j - 1))
                for q in range(QUAD):
                    cols = slice(q * P, (q + 1) * P)
                    for part in range(2):
                        last = nc.tensor.matmul(out_ps[:, cols], hT[:, place[LAYERS], j, part, cols], ident16[:, :],
                                                start=(part == 0), stop=(part == 1))
                last.then_inc(out_turned, 1)

            def slot(kind, b, t):
                if live(kind, t):
                    l, j = layer_tile(t)
                    state, wi, agg = hT[:, l, j], wgi[:, l], aggT[:, t % 2]
                    if l == 0:
                        pe.wait_ge(first_T_ready[j], loads_to(b + t // STEPS))
                    else:
                        pe.wait_ge(lo_ready, steps_to(b, t - TILES))
                    wait(pe, r_ready, steps_to(b, t - 1))
                    product(r_ps, whh, state, 0, last=False)
                    wait(pe, rgh_ready, steps_to(b, t - 1))
                    product(hn_ps, whh, state, 2).then_inc(hn_made, 1)
                    pe.wait_ge(agg_lo_ready, steps_to(b, t))
                    product(r_ps, wi, agg, 0, first=False).then_inc(r_made, 1)
                if live(kind, t):
                    wait(pe, pre_n_ready, steps_to(b, t - 1))
                    product(in_ps, wi, agg, 2).then_inc(in_made, 1)
                if live(kind, t + 1):
                    aggregate(b, t + 1)
                if live(kind, t):
                    wait(pe, z_ready, steps_to(b, t - 1))
                    product(z_ps, whh, state, 1, last=False)
                    product(z_ps, wi, agg, 1, first=False).then_inc(z_made, 1)
                if kind == TAIL and live(kind, t - 2) and layer_tile(t - 2)[0] + 1 == LAYERS:
                    turn_out(b, layer_tile(t - 2)[1])

            pe.wait_ge(weights_loaded, 48)
            pe.wait_ge(ident_made, 2)
            for source, target in ((wih_raw, r_ps), (w_raw, z_ps), (whh_raw, hn_ps)):
                for c in range(3):
                    last = nc.tensor.transpose(target[:, c * P:(c + 1) * P], source[:, c, :], ident32[:, :])
                last.then_inc(w_turned, 1)

            def fold(l):
                nc.tensor.matmul(fold_ps[:, l % 2, 0:GATES * P], wT[:, l, :], wihT[:, :],
                                 start=True, stop=True).then_inc(w_folded, 1)

            pe.wait_ge(w_copied, 2)
            fold(0)
            aggregate(0, 0)
            pe.wait_ge(wlo_ready, 2)
            slot(HEAD, 0, 0)
            fold(1)
            fold(2)
            slot(HEAD, 0, 1)
            slot(HEAD, 0, 2)
            pe.wait_ge(wlo_ready, 4)
            with pe.Fori(0, batches - 1) as b:
                for t in range(LEAD, LEAD + STEPS):
                    slot(BODY, b, t)
            for t in range(LEAD, LEAD + STEPS):
                slot(TAIL, batches - 1, t)

        @block.scalar
        def _(act):
            def first_hi(b, j):
                act.wait_ge(normed_ready, tiles_to(b, j))
                nc.scalar.activation(nat[:, 0, j, 0, :], normed[:, j % 2, :], ACT.Relu).then_inc(first_hi_ready, 1)

            def sign_adj(b, j):
                act.wait_ge(adj_loaded[j], loads_to(b))
                nc.scalar.activation(adj16[:, j, :, :].rearrange("p q t -> p (q t)"), adj_raw[:, j, :],
                                     ACT.Sign).then_inc(sign_made, 1)

            def square_adj(b, j):
                act.wait_ge(sign_made, tiles_to(b - 1, j))
                nc.scalar.activation(adj16[:, j, :, :], adj16[:, j, :, :], ACT.Square).then_inc(adj_ready, 1)

            def agg_hi(b, t):
                act.wait_ge(agg_made, steps_to(b, t))
                nc.scalar.activation(aggT[:, t % 2, 0, :], agg_ps[:, :], ACT.Copy).then_inc(agg_hi_ready, 1)

            def slot(kind, b, t):
                if live(kind, t - 1):
                    act.wait_ge(z_made, steps_to(b, t - 1))
                    nc.scalar.activation(z_buf[:, (t - 1) % 2, :], z_ps[:, :], ACT.Sigmoid,
                                         bias=bias_rz[:, 1:2], scale=1 / WSCALE).then_inc(z_ready, 1)
                if live(kind, t - 2):
                    l, j = layer_tile(t - 2)
                    act.wait_ge(h32_ready, steps_to(b, t - 2))
                    nc.scalar.activation(hT[:, place[l + 1], j, 0, :], h32[:, place[l + 1], j, :],
                                         ACT.Copy).then_inc(hi_ready, 1)
                if live(kind, t):
                    act.wait_ge(r_made, steps_to(b, t))
                    nc.scalar.activation(r_buf[:, t % 2, :], r_ps[:, :], ACT.Sigmoid,
                                         bias=bias_rz[:, 0:1], scale=1 / WSCALE).then_inc(r_ready, 1)
                if t in APPLY_AT[kind]:
                    first_hi(prepared(kind, b), APPLY_AT[kind][t])
                if live(kind, t + 1):
                    agg_hi(b, t + 1)
                if kind == BODY and t in CAST_AT[kind]:
                    sign_adj(b + 1, CAST_AT[kind][t])
                if live(kind, t):
                    act.wait_ge(pre_n_ready, steps_to(b, t))
                    nc.scalar.activation(n_buf[:, t % 2, :], r_buf[:, t % 2, :], ACT.Tanh,
                                         bias=bias_i[:, 2:3], scale=1 / WSCALE).then_inc(n_ready, 1)
                if kind == BODY and t in CAST_AT[kind]:
                    square_adj(b + 1, CAST_AT[kind][t])

            for dst, src in ((wih_raw, w_ih), (whh_raw, w_hh)):
                act.dma_start(dst[:, :, :], src.rearrange("(c g) e -> g c e", c=GATES)).then_inc(weights_loaded, 16)
            act.dma_start(w_raw[:, :, :], weight.rearrange("l d e -> d l e")).then_inc(weights_loaded, 16)
            with nc.allow_non_contiguous_dma("two vectors of 384 values"):
                for dst, src in ((bias_i, b_ih), (bias_h, b_hh)):
                    act.dma_start(dst[:, :], src.rearrange("(c g) -> g c", c=GATES)).then_inc(biases_loaded, 16)
            act.wait_ge(const_made, 2)
            nc.scalar.activation(warm[:, :], eps[:, 0:1], ACT.Sigmoid)
            act.wait_ge(w_turned, 1)
            nc.scalar.activation(wihT[:, :], r_ps[:, 0:GATES * P], ACT.Copy).then_inc(w_copied, 1)
            act.wait_ge(w_turned, 2)
            nc.scalar.activation(wT[:, :, :], z_ps[:, 0:LAYERS * P].rearrange("p (l d) -> p l d", l=LAYERS),
                                 ACT.Copy).then_inc(w_copied, 1)

            def whh_hi():
                act.wait_ge(w_turned, 3)
                nc.scalar.activation(whh[:, 0, :], hn_ps[:, 0:GATES * P], ACT.Copy, scale=WSCALE).then_inc(whi_ready, 1)

            def wgi_hi(l):
                act.wait_ge(w_folded, l + 1)
                nc.scalar.activation(wgi[:, l, 0, :], fold_ps[:, l % 2, 0:GATES * P], ACT.Copy,
                                     scale=WSCALE).then_inc(whi_ready, 1)

            first_hi(0, 0)
            whh_hi()
            first_hi(0, 1)
            wgi_hi(0)
            agg_hi(0, 0)
            act.wait_ge(bias_ready, 1)
            slot(HEAD, 0, 0)
            wgi_hi(1)
            slot(HEAD, 0, 1)
            wgi_hi(2)
            slot(HEAD, 0, 2)
            with act.Fori(0, batches - 1) as b:
                for t in range(LEAD, LEAD + STEPS):
                    slot(BODY, b, t)
            for t in range(LEAD, LEAD + STEPS):
                slot(TAIL, batches - 1, t)

        @block.vector
        def _(dve):
            def half_moments(b, j):
                dve.wait_ge(x_loaded[j], loads_to(b))
                for q in range(QUAD):
                    last = nc.vector.bn_stats(stats[:, j % 2, q, :], x_all[:, bass.ds(b * (TILES * TILE) + (j * TILE + q * P), P)])
                last.then_inc(stats_made, 1)

            def moments(j):
                for q in range(QUAD):
                    last = nc.vector.bn_aggr(mean_var[:, j % 2, q, :], stats[:, j % 2, q, :])
                last.then_inc(moments_ready, 1)

            def norm(b, j):
                dve.wait_ge(rstd_ready, tiles_to(b, j))
                for q in range(QUAD):
                    last = nc.vector.tensor_scalar(
                        normed[:, j % 2, q * P:(q + 1) * P],
                        x_all[:, bass.ds(b * (TILES * TILE) + (j * TILE + q * P), P)],
                        mean_var[:, j % 2, q, 0:1], rstd[:, j % 2, q:q + 1], ALU.subtract, ALU.mult)
                last.then_inc(normed_ready, 1)

            def first_lo(b, j):
                dve.wait_ge(first_hi_ready, tiles_to(b, j))
                nc.vector.scalar_tensor_tensor(nat[:, 0, j, 1, :], normed[:, j % 2, :], 0.0, nat[:, 0, j, 0, :],
                                               ALU.max, ALU.subtract).then_inc(first_lo_ready, 1)

            def cast_adj(b, j):
                dve.wait_ge(adj_loaded[j], loads_to(b))
                nc.vector.tensor_scalar(adj16[:, j, :, :].rearrange("p q t -> p (q t)"), adj_raw[:, j, :], 0.0, None,
                                        ALU.not_equal).then_inc(adj_ready, 1)

            def agg_lo(b, t):
                dve.wait_ge(agg_hi_ready, steps_to(b, t))
                nc.vector.tensor_tensor(aggT[:, t % 2, 1, :], agg_ps[:, :], aggT[:, t % 2, 0, :],
                                        ALU.subtract).then_inc(agg_lo_ready, 1)

            def slot(kind, b, t):
                new = prepared(kind, b)
                if kind == TAIL and live(kind, t - 3) and layer_tile(t - 3)[0] + 1 == LAYERS:
                    j = layer_tile(t - 3)[1]
                    dve.wait_ge(out_turned, j + 1)
                    nc.vector.tensor_tensor(x_tile(b, j), out_ps[:, :], x_tile(b, j), ALU.add).then_inc(added, 1)
                if t in STATS_AT[kind]:
                    half_moments(new, STATS_AT[kind][t])
                if t in APPLY_AT[kind]:
                    norm(new, APPLY_AT[kind][t])
                if kind == HEAD and t in CAST_AT[kind]:
                    cast_adj(new, CAST_AT[kind][t])
                if live(kind, t - 2):
                    l, j = layer_tile(t - 2)
                    dve.wait_ge(hi_ready, steps_to(b, t - 2))
                    nc.vector.tensor_tensor(hT[:, place[l + 1], j, 1, :], h32[:, place[l + 1], j, :],
                                            hT[:, place[l + 1], j, 0, :], ALU.subtract).then_inc(lo_ready, 1)
                if t in STATS_AT[kind]:
                    dve.wait_ge(stats_made, tiles_to(new, STATS_AT[kind][t]))
                if live(kind, t):
                    dve.wait_ge(r_ready, steps_to(b, t))
                    dve.wait_ge(hn_made, steps_to(b, t))
                    nc.vector.scalar_tensor_tensor(r_buf[:, t % 2, :], hn_ps[:, :], bias_hn[:, :], r_buf[:, t % 2, :],
                                                   ALU.add, ALU.mult).then_inc(rgh_ready, 1)
                if t in STATS_AT[kind]:
                    moments(STATS_AT[kind][t])
                if t in APPLY_AT[kind]:
                    first_lo(new, APPLY_AT[kind][t])
                if live(kind, t):
                    dve.wait_ge(in_made, steps_to(b, t))
                    dve.wait_ge(rgh_ready, steps_to(b, t))
                    nc.vector.tensor_tensor(r_buf[:, t % 2, :], in_ps[:, :], r_buf[:, t % 2, :],
                                            ALU.add).then_inc(pre_n_ready, 1)
                if live(kind, t + 1):
                    agg_lo(b, t + 1)
                if live(kind, t - 1):
                    l, j = layer_tile(t - 1)
                    dve.wait_ge(zd_ready, steps_to(b, t - 1))
                    nc.vector.tensor_tensor(h32[:, place[l + 1], j, :], n_buf[:, (t - 1) % 2, :],
                                            d_buf[:, (t - 1) % 2, :], ALU.add).then_inc(h32_ready, 1)
                if kind == BODY and layer_tile(t - 3)[0] + 1 == LAYERS:
                    j = layer_tile(t - 3)[1]
                    dve.wait_ge(hi_added, tiles_to(b, j))
                    nc.vector.tensor_tensor(x_tile(b, j), nat[:, nat_place[LAYERS], j, 1, :], x_tile(b, j),
                                            ALU.add).then_inc(added, 1)

            def moments_of_first(j):
                half_moments(0, j)
                dve.wait_ge(stats_made, tiles_to(0, j))
                moments(j)

            def split_lo(n, target, source):
                dve.wait_ge(whi_ready, n + 1)
                nc.vector.scalar_tensor_tensor(target[:, 1, :], source[:, 0:GATES * P], WSCALE, target[:, 0, :],
                                               ALU.mult, ALU.subtract).then_inc(wlo_ready, 1)

            dve.wait_ge(ident_made, 2)
            nc.vector.tensor_copy(ident16[:, :], ident32[:, :]).then_inc(ident_made, 1)
            moments_of_first(0)
            moments_of_first(1)
            norm(0, 0)
            norm(0, 1)
            first_lo(0, 0)
            split_lo(0, whh, hn_ps)
            first_lo(0, 1)
            cast_adj(0, 0)
            cast_adj(0, 1)
            split_lo(1, wgi[:, 0], fold_ps[:, 0])
            dve.wait_ge(biases_loaded, 32)
            nc.vector.tensor_tensor(bias_rz[:, :], bias_i[:, 0:2], bias_h[:, 0:2], ALU.add)
            nc.vector.tensor_scalar(bias_hn[:, :], bias_h[:, 2:3], WSCALE, None, ALU.mult).then_inc(bias_ready, 1)
            agg_lo(0, 0)
            moments_of_first(2)
            moments_of_first(3)
            slot(HEAD, 0, 0)
            split_lo(2, wgi[:, 1], fold_ps[:, 1])
            slot(HEAD, 0, 1)
            split_lo(3, wgi[:, 2], fold_ps[:, 0])
            slot(HEAD, 0, 2)
            with dve.Fori(0, batches - 1) as b:
                for t in range(LEAD, LEAD + STEPS):
                    slot(BODY, b, t)
            for t in range(LEAD, LEAD + STEPS):
                slot(TAIL, batches - 1, t)

        @block.gpsimd
        def _(pool):
            def inverse_std(b, j):
                pool.wait_ge(moments_ready, tiles_to(b, j))
                nc.gpsimd.tensor_tensor(var_eps[:, j % 2, :], mean_var[:, j % 2, :, 1], eps[:, :],
                                        ALU.add).then_inc(eps_added, 1)
                pool.wait_ge(eps_added, tiles_to(b, j))
                nc.gpsimd.tensor_tensor(rstd[:, j % 2, :], var_eps[:, j % 2, :], minus_half[:, :],
                                        ALU.pow).then_inc(rstd_ready, 1)

            def first_h32(b, j):
                pool.wait_ge(first_T_ready[j], loads_to(b))
                nc.gpsimd.tensor_tensor(h32[:, 0, j, :], hT[:, 0, j, 0, :], hT[:, 0, j, 1, :],
                                        ALU.add).then_inc(first_h32_ready, 1)

            def slot(kind, b, t):
                if live(kind, t - 1):
                    pool.wait_ge(z_ready, steps_to(b, t - 1))
                    pool.wait_ge(d_ready, steps_to(b, t - 1))
                    p = (t - 1) % 2
                    nc.gpsimd.tensor_tensor(d_buf[:, p, :], z_buf[:, p, :], d_buf[:, p, :],
                                            ALU.mult).then_inc(zd_ready, 1)
                if t in STATS_AT[kind]:
                    inverse_std(prepared(kind, b), STATS_AT[kind][t])
                if t in H32_AT[kind]:
                    first_h32(prepared(kind, b), H32_AT[kind][t])
                if kind == BODY and layer_tile(t - 3)[0] + 1 == LAYERS:
                    j = layer_tile(t - 3)[1]
                    pool.wait_ge(nat_ready[j], turns_to(b, t - 3))
                    nc.gpsimd.tensor_tensor(x_tile(b, j), nat[:, nat_place[LAYERS], j, 0, :], x_tile(b, j),
                                            ALU.add).then_inc(hi_added, 1)
                if live(kind, t):
                    l, j = layer_tile(t)
                    pool.wait_ge(n_ready, steps_to(b, t))
                    if l == 0:
                        pool.wait_ge(first_h32_ready, tiles_to(b, t // STEPS * TILES + j))
                    wait(pool, h32_ready, steps_to(b, t - 2))
                    nc.gpsimd.tensor_tensor(d_buf[:, t % 2, :], h32[:, l, j, :], n_buf[:, t % 2, :],
                                            ALU.subtract).then_inc(d_ready, 1)

            nc.gpsimd.memset(ident32[:, :], 0.0).then_inc(ident_made, 1)
            pool.wait_ge(ident_made, 1)
            nc.gpsimd.affine_select(out=ident32[:, :], in_=ident32[:, :], compare_op=ALU.not_equal, fill=1.0,
                                    base=0, pattern=[[-1, P]], channel_multiplier=1).then_inc(ident_made, 1)
            nc.gpsimd.memset(minus_half[:, :], -0.5).then_inc(const_made, 1)
            nc.gpsimd.memset(eps[:, :], EPS).then_inc(const_made, 1)
            pool.wait_ge(const_made, 2)
            for j in range(TILES):
                inverse_std(0, j)
            first_h32(0, 0)
            first_h32(0, 1)
            for t in range(LEAD):
                slot(HEAD, 0, t)
            with pool.Fori(0, batches - 1) as b:
                for t in range(LEAD, LEAD + STEPS):
                    slot(BODY, b, t)
            for t in range(LEAD, LEAD + STEPS):
                slot(TAIL, batches - 1, t)


_INPUTS = ("x", "adj", "L0_gnn_weight", "L0_gnn_w_ih", "L0_gnn_w_hh", "L0_gnn_b_ih", "L0_gnn_b_hh")


def kernel(**inputs):
    import numpy as np
    import concourse.bacc as bacc
    from concourse.bass_utils import run_bass_kernel_spmd

    nc = bacc.Bacc("TRN2", target_bir_lowering=False, num_devices=1)
    arrays, args = {}, []
    for name in _INPUTS:
        a = np.ascontiguousarray(inputs[name])
        arrays[f"in_{name}"] = a
        args.append(nc.dram_tensor(f"in_{name}", a.shape, mybir.dt.from_np(a.dtype), kind="ExternalInput").ap())
    shape = arrays["in_x"].shape
    out = nc.dram_tensor("out", shape, mybir.dt.float32, kind="ExternalOutput").ap()
    gnn_program(nc, *args, out)
    result = run_bass_kernel_spmd(nc, [arrays], core_ids=[0])
    return result.results[0]["out"]
```
